# Optimizing a Trainium2 kernel written in Bass

```python
import numpy as np
import jax
import jax.numpy as jnp

def _softmax(x, axis=-1):
    return jax.nn.softmax(x, axis=axis)

def _gelu(x):
    return jax.nn.gelu(x, approximate=True)

def _silu(x):
    return jax.nn.silu(x)

def _sigmoid(x):
    return jax.nn.sigmoid(x)

def _layernorm(x, axis=-1, eps=1e-05):
    m = jnp.mean(x, axis=axis, keepdims=True)
    v = jnp.var(x, axis=axis, keepdims=True)
    return (x - m) / jnp.sqrt(v + eps)

def _scatter_add(tgt, idx, src, axis=0):
    return tgt.at[idx].add(src)

def _segment_sum(src, seg, n):
    return jax.ops.segment_sum(src, seg, n)
kernel_name = 'mk_dlrm_tower_d1_rec_r8_51092c'

def setup_inputs(seed: int=0):
    np.random.seed(seed)
    _w = jnp.asarray

    def _rec_inputs():
        import jax
        import jax.numpy as jnp
        _tk = jax.random.key(seed)
        ids = jnp.stack([jax.random.randint(jax.random.fold_in(_tk, 200 + f), (512,), 0, v, jnp.int32) for f, v in enumerate([12500, 1000, 12500, 1250, 125000, 1000, 1250, 1000, 12500, 1250, 1250, 1250, 1000, 1250, 12500, 1000, 12500, 12500, 1250, 12500, 1000, 1000, 1000, 1000, 1250, 12500])], axis=1)
        tbl_0 = 0.05 * jax.random.normal(jax.random.fold_in(_tk, 500 + 0), (12500, 128), jnp.float32)
        tbl_1 = 0.05 * jax.random.normal(jax.random.fold_in(_tk, 500 + 1), (1000, 128), jnp.float32)
        tbl_2 = 0.05 * jax.random.normal(jax.random.fold_in(_tk, 500 + 2), (12500, 128), jnp.float32)
        tbl_3 = 0.05 * jax.random.normal(jax.random.fold_in(_tk, 500 + 3), (1250, 128), jnp.float32)
        tbl_4 = 0.05 * jax.random.normal(jax.random.fold_in(_tk, 500 + 4), (125000, 128), jnp.float32)
        tbl_5 = 0.05 * jax.random.normal(jax.random.fold_in(_tk, 500 + 5), (1000, 128), jnp.float32)
        tbl_6 = 0.05 * jax.random.normal(jax.random.fold_in(_tk, 500 + 6), (1250, 128), jnp.float32)
        tbl_7 = 0.05 * jax.random.normal(jax.random.fold_in(_tk, 500 + 7), (1000, 128), jnp.float32)
        tbl_8 = 0.05 * jax.random.normal(jax.random.fold_in(_tk, 500 + 8), (12500, 128), jnp.float32)
        tbl_9 = 0.05 * jax.random.normal(jax.random.fold_in(_tk, 500 + 9), (1250, 128), jnp.float32)
        tbl_10 = 0.05 * jax.random.normal(jax.random.fold_in(_tk, 500 + 10), (1250, 128), jnp.float32)
        tbl_11 = 0.05 * jax.random.normal(jax.random.fold_in(_tk, 500 + 11), (1250, 128), jnp.float32)
        tbl_12 = 0.05 * jax.random.normal(jax.random.fold_in(_tk, 500 + 12), (1000, 128), jnp.float32)
        tbl_13 = 0.05 * jax.random.normal(jax.random.fold_in(_tk, 500 + 13), (1250, 128), jnp.float32)
        tbl_14 = 0.05 * jax.random.normal(jax.random.fold_in(_tk, 500 + 14), (12500, 128), jnp.float32)
        tbl_15 = 0.05 * jax.random.normal(jax.random.fold_in(_tk, 500 + 15), (1000, 128), jnp.float32)
        tbl_16 = 0.05 * jax.random.normal(jax.random.fold_in(_tk, 500 + 16), (12500, 128), jnp.float32)
        tbl_17 = 0.05 * jax.random.normal(jax.random.fold_in(_tk, 500 + 17), (12500, 128), jnp.float32)
        tbl_18 = 0.05 * jax.random.normal(jax.random.fold_in(_tk, 500 + 18), (1250, 128), jnp.float32)
        tbl_19 = 0.05 * jax.random.normal(jax.random.fold_in(_tk, 500 + 19), (12500, 128), jnp.float32)
        tbl_20 = 0.05 * jax.random.normal(jax.random.fold_in(_tk, 500 + 20), (1000, 128), jnp.float32)
        tbl_21 = 0.05 * jax.random.normal(jax.random.fold_in(_tk, 500 + 21), (1000, 128), jnp.float32)
        tbl_22 = 0.05 * jax.random.normal(jax.random.fold_in(_tk, 500 + 22), (1000, 128), jnp.float32)
        tbl_23 = 0.05 * jax.random.normal(jax.random.fold_in(_tk, 500 + 23), (1000, 128), jnp.float32)
        tbl_24 = 0.05 * jax.random.normal(jax.random.fold_in(_tk, 500 + 24), (1250, 128), jnp.float32)
        tbl_25 = 0.05 * jax.random.normal(jax.random.fold_in(_tk, 500 + 25), (12500, 128), jnp.float32)
        _rk = jax.random.fold_in(_tk, 7)
        r_dense_features = -0.000292821 + 1.00034 * jax.random.normal(jax.random.fold_in(_rk, 101), (512, 128), jnp.float32)
        W_top1 = 0.0405887 * jax.random.normal(jax.random.fold_in(_tk, 801), (607, 512), jnp.float32)
        W_top2 = 0.0441942 * jax.random.normal(jax.random.fold_in(_tk, 802), (512, 256), jnp.float32)
        W_top3 = 0.0625 * jax.random.normal(jax.random.fold_in(_tk, 803), (256, 1), jnp.float32)
        b_top1 = jnp.zeros((512,), jnp.float32)
        b_top2 = jnp.zeros((256,), jnp.float32)
        return (r_dense_features, ids, tbl_0, tbl_1, tbl_2, tbl_3, tbl_4, tbl_5, tbl_6, tbl_7, tbl_8, tbl_9, tbl_10, tbl_11, tbl_12, tbl_13, tbl_14, tbl_15, tbl_16, tbl_17, tbl_18, tbl_19, tbl_20, tbl_21, tbl_22, tbl_23, tbl_24, tbl_25, W_top1, b_top1, W_top2, b_top2, W_top3)
    r_dense_features, ids, tbl_0, tbl_1, tbl_2, tbl_3, tbl_4, tbl_5, tbl_6, tbl_7, tbl_8, tbl_9, tbl_10, tbl_11, tbl_12, tbl_13, tbl_14, tbl_15, tbl_16, tbl_17, tbl_18, tbl_19, tbl_20, tbl_21, tbl_22, tbl_23, tbl_24, tbl_25, W_top1, b_top1, W_top2, b_top2, W_top3 = _rec_inputs()

    def _L0_rec_setup():
        import jax, jax.numpy as jnp
        import numpy as np
        F = 26
        _TRIU_I, _TRIU_J = np.triu_indices(F + 1, k=1)
        key = jax.random.key(seed)
        k1, k2 = jax.random.split(key)
        B, D = (4096, 128)
        dense_features = jax.random.normal(k1, (B, D), dtype=jnp.float32)
        sparse_features = jax.random.normal(k2, (B, F, D), dtype=jnp.float32)
        return {'dense_features': dense_features, 'sparse_features': sparse_features}
    _L0_rec_all = _L0_rec_setup()
    _L0_rec_in = {k: v for k, v in _L0_rec_all.items() if k in ()}
    del _L0_rec_all
    return {'r_dense_features': r_dense_features, 'ids': ids, 'tbl_0': tbl_0, 'tbl_1': tbl_1, 'tbl_2': tbl_2, 'tbl_3': tbl_3, 'tbl_4': tbl_4, 'tbl_5': tbl_5, 'tbl_6': tbl_6, 'tbl_7': tbl_7, 'tbl_8': tbl_8, 'tbl_9': tbl_9, 'tbl_10': tbl_10, 'tbl_11': tbl_11, 'tbl_12': tbl_12, 'tbl_13': tbl_13, 'tbl_14': tbl_14, 'tbl_15': tbl_15, 'tbl_16': tbl_16, 'tbl_17': tbl_17, 'tbl_18': tbl_18, 'tbl_19': tbl_19, 'tbl_20': tbl_20, 'tbl_21': tbl_21, 'tbl_22': tbl_22, 'tbl_23': tbl_23, 'tbl_24': tbl_24, 'tbl_25': tbl_25, 'W_top1': W_top1, 'b_top1': b_top1, 'W_top2': W_top2, 'b_top2': b_top2, 'W_top3': W_top3}

def reference(r_dense_features, ids, tbl_0, tbl_1, tbl_2, tbl_3, tbl_4, tbl_5, tbl_6, tbl_7, tbl_8, tbl_9, tbl_10, tbl_11, tbl_12, tbl_13, tbl_14, tbl_15, tbl_16, tbl_17, tbl_18, tbl_19, tbl_20, tbl_21, tbl_22, tbl_23, tbl_24, tbl_25, W_top1, b_top1, W_top2, b_top2, W_top3):
    import jax
    import jax.numpy as jnp

    def _L0_rec_ref(dense_features, sparse_features):
        import jax, jax.numpy as jnp
        import numpy as np
        F = 26
        _TRIU_I, _TRIU_J = np.triu_indices(F + 1, k=1)
        combined = jnp.concatenate([dense_features[:, None, :], sparse_features], axis=1)
        interactions = jnp.einsum('bfd,bgd->bfg', combined, combined)
        interactions_flat = interactions[:, _TRIU_I, _TRIU_J]
        return jnp.concatenate([dense_features, interactions_flat], axis=1)
    e = jnp.stack([tbl_0[ids[:, 0]], tbl_1[ids[:, 1]], tbl_2[ids[:, 2]], tbl_3[ids[:, 3]], tbl_4[ids[:, 4]], tbl_5[ids[:, 5]], tbl_6[ids[:, 6]], tbl_7[ids[:, 7]], tbl_8[ids[:, 8]], tbl_9[ids[:, 9]], tbl_10[ids[:, 10]], tbl_11[ids[:, 11]], tbl_12[ids[:, 12]], tbl_13[ids[:, 13]], tbl_14[ids[:, 14]], tbl_15[ids[:, 15]], tbl_16[ids[:, 16]], tbl_17[ids[:, 17]], tbl_18[ids[:, 18]], tbl_19[ids[:, 19]], tbl_20[ids[:, 20]], tbl_21[ids[:, 21]], tbl_22[ids[:, 22]], tbl_23[ids[:, 23]], tbl_24[ids[:, 24]], tbl_25[ids[:, 25]]], axis=1)
    z = _L0_rec_ref(r_dense_features, e)
    z = z.reshape(z.shape[0], -1)
    h = jnp.concatenate([z, r_dense_features], axis=1)
    h = jnp.maximum(h @ W_top1 + b_top1, 0.0)
    h = jnp.maximum(h @ W_top2 + b_top2, 0.0)
    y = h @ W_top3
    return y

_drawn_inputs = setup_inputs


def setup_inputs(seed=0):
    import zlib

    import numpy as np

    out = dict(_drawn_inputs(seed))
    spreads = {'b_top1': (0.0, 0.1), 'b_top2': (0.0, 0.1)}
    factors = {}
    for name, (base, spread) in spreads.items():
        noise = np.random.default_rng([zlib.crc32(name.encode()), seed]).standard_normal(out[name].shape)
        drawn = base * np.exp(spread * noise) if base else spread * noise
        out[name] = jnp.asarray(drawn.astype(out[name].dtype))
    for name, factor in factors.items():
        out[name] = (out[name] * factor).astype(out[name].dtype)
    return out
```

```python
from contextlib import ExitStack

import concourse.bass as bass
from concourse import mybir

P = 128
NT = 26
F = NT + 1
FP = 32
D = 128
TB = 128
TG = 4
NG = -(-F // TG)
Q = 4
M = -(-NT // Q)
GC = Q * NT
GB = 4
GK = 2
GS = GK * GB * Q
NR = TB // GS
H1, H2 = 512, 256
N1, N2 = H1 // P, H2 // P

ALU = mybir.AluOpType
ACT = mybir.ActivationFunctionType
F32 = mybir.dt.float32
I32 = mybir.dt.int32
U32 = mybir.dt.uint32


def dlrm_tower(nc, dense, ids, tables, w_dense, w_pairs, w2, w3, b1, b2, out):
    B = dense.shape[0]
    T = B // TB
    with ExitStack() as ctx:
        def sb(name, shape, dt=F32):
            return ctx.enter_context(nc.sbuf_tensor(name, shape, dt))

        def ps(name, shape):
            return ctx.enter_context(nc.psum_tensor(name, shape, F32))

        def sem(name):
            return ctx.enter_context(nc.semaphore(name))

        ids_sb = [sb(f"ids_sb{i}", [P, NT], I32) for i in range(2)]
        X = [sb(f"X{i}", [P, F, D]) for i in range(2)]
        XT = sb("XT", [P, TB, FP])
        denseT = sb("denseT", [P, TB])
        Z = sb("Z", [P, M, TB])
        w_dense_sb = sb("w_dense_sb", [P, 2, H1])
        wd = sb("wd", [P, H1])
        w_pairs_sb = sb("w_pairs_sb", [P, M, H1])
        w2_sb = sb("w2_sb", [P, N1, H2])
        w3_sb = sb("w3_sb", [P, N2])
        b1_sb = sb("b1_sb", [P, N1])
        b2_sb = sb("b2_sb", [P, N2])
        h1 = sb("h1", [P, N1, TB])
        h2 = sb("h2", [P, N2, TB])
        y = sb("y", [1, B])
        ident = sb("ident", [P, P])

        pT = [ps(f"pT{k}", [P, TG, TB]) for k in range(2)]
        pG = [ps(f"pG{s}", [P, GK, 512]) for s in range(2)]
        p1 = ps("p1", [P, N1, TB])
        p2 = ps("p2", [P, 512])
        p2v = p2[:, 0:N2 * TB].rearrange("p (n b) -> p n b", n=N2)
        pY = p2[0:1, N2 * TB:N2 * TB + TB]

        ids_in = [sem(f"ids_in{i}") for i in range(2)]
        dense_in = [sem(f"dense_in{i}") for i in range(2)]
        gathered = [[sem(f"gathered{i}_{g}") for g in range(NG)] for i in range(2)]
        wd_in = sem("wd_in")
        w1_in = sem("w1_in")
        rest_in = sem("rest_in")
        zeroed = sem("zeroed")
        ident_ready = sem("ident_ready")
        pads_ready = sem("pads_ready")
        wd_ready = sem("wd_ready")
        transposed = [sem(f"transposed{k}") for k in range(2)]
        xt_copied = [sem(f"xt_copied{k}") for k in range(2)]
        x_read = [sem(f"x_read{i}") for i in range(2)]
        gram_done = [sem(f"gram_done{s}") for s in range(2)]
        z_dve = [sem(f"z_dve{s}") for s in range(2)]
        z_act = [sem(f"z_act{s}") for s in range(2)]
        l1_done = sem("l1_done")
        h1_ready = sem("h1_ready")
        l2_done = sem("l2_done")
        h2_ready = sem("h2_ready")
        l3_done = sem("l3_done")
        y_ready = sem("y_ready")
        stored = sem("stored")

        def copy_granule(copy, s, r, samples):
            for j in samples:
                src = pG[s][32 * j:32 * j + 32, :, 0:GB * GC].rearrange("p k (u c) -> p k u c", c=GC)
                dst = Z[:, :, r * GS:(r + 1) * GS].rearrange("p m (k u j) -> p k u m j", k=GK, j=Q)
                for q in range(Q):
                    mq = len(range(q, NT, Q))
                    last = copy(dst[32 * q:32 * q + 32, :, :, 0:mq, j], src[:, :, :, j * NT + q:(j + 1) * NT:Q])
            return last

        block = ctx.enter_context(nc.Block())

        @block.sync
        def _(sp):
            for par in range(2):
                sp.dma_start(ids_sb[par][:], ids[par * TB:(par + 1) * TB, :]).then_inc(ids_in[par], 16)
            sp.dma_start(X[0][:, 0, :], dense[0:TB, :]).then_inc(dense_in[0], 16)
            sp.dma_start(X[1][:, 0, :], dense[TB:2 * TB, :]).then_inc(dense_in[1], 16)
            sp.dma_start(w_dense_sb[:], w_dense).then_inc(wd_in, 16)
            sp.dma_start(w_pairs_sb[:], w_pairs).then_inc(w1_in, 16)
            sp.dma_start(w2_sb[:], w2).then_inc(rest_in, 16)
            sp.dma_start(w3_sb[:], w3).then_inc(rest_in, 16)
            sp.dma_start(b1_sb[:], b1).then_inc(rest_in, 16)
            sp.dma_start(b2_sb[:], b2).then_inc(rest_in, 16)
            with sp.Fori(1, T // 2) as i:
                for par in range(2):
                    sp.wait_ge(x_read[par], i)
                    sp.dma_start(ids_sb[par][:], ids[bass.ds((2 * i + par) * TB, TB), :]).then_inc(ids_in[par], 16)
                    sp.dma_start(X[par][:, 0, :], dense[bass.ds((2 * i + par) * TB, TB), :]).then_inc(dense_in[par], 16)
            sp.wait_ge(y_ready, T + 1)
            sp.dma_start(out.rearrange("b o -> o b"), y[:]).then_inc(stored, 16)
            sp.wait_ge(stored, 16)

        @block.gpsimd
        def _(pool):
            pool.memset(ident[:], 0.0).then_inc(zeroed, 1)
            pool.wait_ge(zeroed, 1)
            pool.affine_select(out=ident[:], in_=ident[:], compare_op=ALU.not_equal, fill=1.0, base=0,
                               pattern=[[-1, P]], channel_multiplier=1).then_inc(ident_ready, 1)
            for t in range(T):
                par = t % 2
                if t >= 2:
                    pool.wait_ge(x_read[par], t // 2)
                pool.wait_ge(ids_in[par], 16 * (t // 2 + 1))
                for f in range(NT):
                    at = ids_sb[par][:, f:f + 1].bitcast(U32)
                    pool.indirect_dma_start(X[par][:, 1 + f, :], None, tables[f], bass.IndirectOffsetOnAxis(at, 0)) \
                        .then_inc(gathered[par][(1 + f) // TG], 16)

        @block.vector
        def _(dve):
            for n in range(2):
                dve.sem_inc(xt_copied[n], 1)
                dve.sem_inc(z_dve[n], 1)
            dve.memset(XT[:, :, F:FP], 0.0).then_inc(pads_ready, 1)
            dve.memset(Z[:, M - 1, :], 0.0).then_inc(pads_ready, 1)
            dve.wait_ge(wd_in, 16)
            dve.tensor_tensor(wd[:], w_dense_sb[:, 0, :], w_dense_sb[:, 1, :], ALU.add).then_inc(wd_ready, 1)
            dve.wait_ge(pads_ready, 2)
            with dve.Fori(0, T // 2) as i:
                for par in range(2):
                    t = 2 * i + par
                    for g in range(NG):
                        c = NG * par + g
                        k, n = c % 2, min(TG, F - TG * g)
                        dve.wait_ge(transposed[k], NG * i + c // 2 + 1)
                        if g == 0:
                            dve.tensor_copy(denseT[:], pT[k][:, 0, :])
                        dve.tensor_copy(XT[:, :, TG * g:TG * g + n].rearrange("p b f -> p f b"),
                                        pT[k][:, 0:n, :]).then_inc(xt_copied[k], 1)
                    for r in range(NR):
                        s = r % 2
                        dve.wait_ge(gram_done[s], NR // 2 * t + r // 2 + 1)
                        copy_granule(dve.tensor_copy, s, r, (0, 1)).then_inc(z_dve[s], 1)

        @block.scalar
        def _(act):
            for free in (*z_act, h1_ready, y_ready):
                act.sem_inc(free, 1)
            act.wait_ge(pads_ready, 2)
            act.wait_ge(rest_in, 64)
            with act.Fori(0, T // 2) as i:
                for par in range(2):
                    t = 2 * i + par
                    for r in range(NR):
                        s = r % 2
                        act.wait_ge(gram_done[s], NR // 2 * t + r // 2 + 1)
                        copy_granule(act.copy, s, r, (2, 3)).then_inc(z_act[s], 1)
                    act.wait_ge(l1_done, t + 1)
                    for n in range(N1):
                        last = act.activation(h1[:, n, :], p1[:, n, :], ACT.Relu, bias=b1_sb[:, n:n + 1])
                    last.then_inc(h1_ready, 1)
                    act.wait_ge(l2_done, t + 1)
                    for n in range(N2):
                        last = act.activation(h2[:, n, :], p2v[:, n, :], ACT.Relu, bias=b2_sb[:, n:n + 1])
                    last.then_inc(h2_ready, 1)
                    act.wait_ge(l3_done, t + 1)
                    act.copy(y[:, bass.ds(t * TB, TB)], pY).then_inc(y_ready, 1)

        @block.tensor
        def _(pe):
            pe.wait_ge(ident_ready, 1)
            pe.wait_ge(pads_ready, 2)
            pe.wait_ge(wd_ready, 1)
            pe.wait_ge(w1_in, 16)
            pe.wait_ge(rest_in, 64)
            with pe.Fori(0, T // 2) as i:
                for par in range(2):
                    t = 2 * i + par
                    pe.wait_ge(dense_in[par], 16 * (i + 1))
                    for g in range(NG):
                        c = NG * par + g
                        k, n = c % 2, min(TG, F - TG * g)
                        pe.wait_ge(gathered[par][g], 16 * (n - (g == 0)) * (i + 1))
                        pe.wait_ge(xt_copied[k], NG * i + c // 2 + 1)
                        for f in range(n):
                            last = pe.transpose(pT[k][:, f, :], X[par][:, TG * g + f, :], ident[:])
                        last.then_inc(transposed[k], 1)
                    for k in range(2):
                        pe.wait_ge(xt_copied[k], NG * i + (NG * (par + 1) + 1 - k) // 2 + 1)
                    for r in range(NR):
                        s = r % 2
                        pe.wait_ge(z_dve[s], NR // 2 * t + r // 2 + 1)
                        pe.wait_ge(z_act[s], NR // 2 * t + r // 2 + 1)
                        for u in range(GK * GB):
                            b = r * GS + u * Q
                            last = pe.matmul(pG[s][:, u // GB, u % GB * GC:(u % GB + 1) * GC],
                                             XT[:, b:b + Q, :].rearrange("p b f -> p (b f)"),
                                             XT[:, b:b + Q, 1:F], start=True, stop=True)
                            if r == 0 and u == 0:
                                last.then_inc(x_read[par], 1)
                        last.then_inc(gram_done[s], 1)
                    for s in range(2):
                        pe.wait_ge(z_dve[s], NR // 2 * (t + 1) + 1)
                        pe.wait_ge(z_act[s], NR // 2 * (t + 1) + 1)
                    pe.wait_ge(h1_ready, t + 1)
                    for n in range(N1):
                        cols = slice(n * P, (n + 1) * P)
                        pe.matmul(p1[:, n, :], wd[:, cols], denseT[:], start=True, stop=False)
                        for m in range(M):
                            last = pe.matmul(p1[:, n, :], w_pairs_sb[:, m, cols], Z[:, m, :],
                                             start=False, stop=(m == M - 1))
                    last.then_inc(l1_done, 1)
                    pe.wait_ge(h1_ready, t + 2)
                    for n in range(N2):
                        for m in range(N1):
                            last = pe.matmul(p2v[:, n, :], w2_sb[:, m, n * P:(n + 1) * P], h1[:, m, :],
                                             start=(m == 0), stop=(m == N1 - 1))
                    last.then_inc(l2_done, 1)
                    pe.wait_ge(h2_ready, t + 1)
                    pe.wait_ge(y_ready, t + 1)
                    for m in range(N2):
                        last = pe.matmul(pY, w3_sb[:, m:m + 1], h2[:, m, :], start=(m == 0), stop=(m == N2 - 1))
                    last.then_inc(l3_done, 1)


def kernel(**inputs):
    import numpy as np
    import concourse.bacc as bacc
    from concourse.bass_utils import run_bass_kernel_spmd

    ids = np.asarray(inputs["ids"])
    w1 = np.asarray(inputs["W_top1"])
    B = ids.shape[0]
    none = w1.shape[0]
    row = np.full((P, M), none)
    for g in range(1, F):
        for f in range(g):
            m, q = divmod(g - 1, Q)
            row[32 * q + f, m] = D + f * (2 * F - f - 1) // 2 + g - f - 1
    padded = np.concatenate([w1, np.zeros((1, H1), w1.dtype)])
    arrays = {
        "dense": np.asarray(inputs["r_dense_features"]),
        "ids": ids,
        "w_dense": np.stack([w1[0:D], w1[none - D:none]], axis=1),
        "w_pairs": padded[row],
        "w2": np.asarray(inputs["W_top2"]).reshape(N1, P, H2).transpose(1, 0, 2),
        "w3": np.asarray(inputs["W_top3"]).reshape(N2, P).T,
        "b1": np.asarray(inputs["b_top1"]).reshape(N1, P).T,
        "b2": np.asarray(inputs["b_top2"]).reshape(N2, P).T,
    }
    for f in range(NT):
        arrays[f"tbl_{f}"] = np.asarray(inputs[f"tbl_{f}"])
    arrays = {f"in_{k}": np.ascontiguousarray(a) for k, a in arrays.items()}
    nc = bacc.Bacc("TRN2", target_bir_lowering=False, num_devices=1)
    ap = {k[3:]: nc.dram_tensor(k, a.shape, mybir.dt.from_np(a.dtype), kind="ExternalInput").ap()
          for k, a in arrays.items()}
    out = nc.dram_tensor("out_y", (B, 1), F32, kind="ExternalOutput").ap()
    dlrm_tower(nc, ap["dense"], ap["ids"], [ap[f"tbl_{f}"] for f in range(NT)], ap["w_dense"], ap["w_pairs"],
               ap["w2"], ap["w3"], ap["b1"], ap["b2"], out)
    return run_bass_kernel_spmd(nc, [arrays], core_ids=[0]).results[0]["out_y"]
```

```python
from contextlib import ExitStack

import concourse.bass as bass
from concourse import mybir

P = 128
NT = 26
F = NT + 1
FP = 32
D = 128
TB = 128
H1, H2 = 512, 256
N1, N2 = H1 // P, H2 // P

SEL = [1, 5, 7, 12, 15]
NS = len(SEL)
GAT = [f for f in range(NT) if f not in SEL]
RP, RC = 125, 8
ACT_ROWS = 2
SLOTS = [1 + f for f in SEL] + [0] + [1 + f for f in GAT]

Q = 4
GC = Q * NT
M = -(-NT // Q)
GK = 2
GU = 4
GS = GK * GU * Q
NR = TB // GS

TG = 4
NX = 1 + len(GAT)
NG = 6
FIRST = [[]] * (NS - 1) + [list(range(NG))]
GROUPS = [(x, min(TG, NX - x)) for x in range(0, NX, TG)]
assert len(GROUPS) == NG and NG % 2 == 0 and NR % 2 == 0

ALU = mybir.AluOpType
ACT = mybir.ActivationFunctionType
F32 = mybir.dt.float32
F32R = mybir.dt.float32r
I32 = mybir.dt.int32
U32 = mybir.dt.uint32


def dlrm_tower(nc, dense, ids, picks, tables, w_dense, w_pairs, w2, w3, b1, b2, out):
    B = dense.shape[0]
    T = B // TB
    with ExitStack() as ctx:
        def sb(name, shape, dt=F32):
            return ctx.enter_context(nc.sbuf_tensor(name, shape, dt))

        def ps(name, shape):
            return ctx.enter_context(nc.psum_tensor(name, shape, F32))

        def sem(name):
            return ctx.enter_context(nc.semaphore(name))

        picks_sb = [sb(f"picks{n}_sb", [P, B], I32) for n in range(NS)]
        table = [sb(f"table{n}", [RP, RC, D]) for n in range(NS)]
        t_hi = [sb(f"t_hi{n}", [RP, RC, D], F32R) for n in range(2)]
        t_lo = [sb(f"t_lo{n}", [RP, RC, D], F32R) for n in range(2)]
        onehot = [sb(f"onehot{n}", [RP, RC, B], F32R) for n in range(2)]
        away = [sb(f"away{n}", [RP, ACT_ROWS, B]) for n in range(2)]
        rows_i = sb("rows_i", [P, RC], I32)
        rows = sb("rows", [P, RC])
        rows_neg = sb("rows_neg", [P, RC])
        picked = sb("picked", [P, NS, B])
        ids_sb = sb("ids_sb", [P, T, NT], I32)
        X = [sb(f"X{i}", [P, NX, D]) for i in range(2)]
        XT = sb("XT", [P, TB, FP])
        denseT = [sb(f"denseT{i}", [P, TB]) for i in range(2)]
        Z = sb("Z", [P, M, TB])
        h1 = sb("h1", [P, N1, TB])
        h2 = sb("h2", [P, N2, TB])
        y = sb("y", [1, B])
        w_dense_sb = sb("w_dense_sb", [P, 2, H1])
        wd = sb("wd", [P, H1])
        w_pairs_sb = sb("w_pairs_sb", [P, M, H1])
        w2_sb = sb("w2_sb", [P, N1, H2])
        w3_sb = sb("w3_sb", [P, N2])
        b1_sb = sb("b1_sb", [P, N1])
        b2_sb = sb("b2_sb", [P, N2])
        ident = sb("ident", [P, P])

        pT = [ps(f"pT{k}", [P, TG, TB]) for k in range(2)]
        pG = [ps(f"pG{s}", [P, GK, 512]) for s in range(2)]
        p1 = [ps("p1_first", [P, N1 - 1, TB]), ps("p1_last", [P, 1, TB])]
        p2 = [pG[0][:, n, 0:TB] for n in range(N2)]
        pY = pG[1][0:1, 0, 0:TB]

        ids_in = sem("ids_in")
        dense_in = [sem(f"dense_in{i}") for i in range(2)]
        gathered = [[sem(f"gathered{i}_{g}") for g in range(NG)] for i in range(2)]
        picks_in = [sem(f"picks_in{n}") for n in range(NS)]
        table_in = [sem(f"table_in{n}") for n in range(NS)]
        wd_in = sem("wd_in")
        w1_in = sem("w1_in")
        rest_in = sem("rest_in")
        zeroed = sem("zeroed")
        ident_ready = sem("ident_ready")
        rows_made = sem("rows_made")
        rows_ready = sem("rows_ready")
        rows_neg_ready = sem("rows_neg_ready")
        pads_ready = sem("pads_ready")
        wd_ready = sem("wd_ready")
        hi_ready = sem("hi_ready")
        away_ready = sem("away_ready")
        onehot_dve = sem("onehot_dve")
        onehot_act = sem("onehot_act")
        lo_ready = sem("lo_ready")
        picked_done = sem("picked_done")
        picked_ready = sem("picked_ready")
        xt_picked = sem("xt_picked")
        transposed = [sem(f"transposed{k}") for k in range(2)]
        xt_copied = [sem(f"xt_copied{k}") for k in range(2)]
        gram_done = [sem(f"gram_done{s}") for s in range(2)]
        z_dve = [sem(f"z_dve{s}") for s in range(2)]
        z_act = [sem(f"z_act{s}") for s in range(2)]
        l1_done = [sem("l1_first_done"), sem("l1_last_done")]
        h1_ready = [sem("h1_first_ready"), sem("h1_last_ready")]
        l2_done = [sem(f"l2_done{n}") for n in range(N2)]
        h2_ready = [sem(f"h2_ready{n}") for n in range(N2)]
        l3_done = sem("l3_done")
        y_ready = sem("y_ready")
        stored = sem("stored")

        def copy_granule(copy, r, samples):
            for j in samples:
                src = pG[r % 2][32 * j:32 * j + 32, :, 0:GU * GC].rearrange("p k (u c) -> p k u c", c=GC)
                dst = Z[:, :, r * GS:(r + 1) * GS].rearrange("p m (k u j) -> p k u m j", k=GK, j=Q)
                for q in range(Q):
                    c = len(range(q, NT, Q))
                    last = copy(dst[32 * q:32 * q + 32, :, :, 0:c, j], src[:, :, :, j * NT + q:(j + 1) * NT:Q])
            return last

        def copy_group(copy, g):
            x, n = GROUPS[g]
            return copy(XT[:, :, NS + x:NS + x + n].rearrange("p b f -> p f b"), pT[g % 2][:, 0:n, :])

        block = ctx.enter_context(nc.Block())

        @block.sync
        def _(sp):
            sp.dma_start(ids_sb[:], ids.rearrange("(t p) f -> p t f", p=TB)).then_inc(ids_in, 16)
            for n in range(NS):
                sp.dma_start(picks_sb[n][:], picks[n, :].partition_broadcast(P)).then_inc(picks_in[n], 16)
                sp.dma_start(table[n][:], tables[SEL[n]].rearrange("(p c) d -> p c d", c=RC)) \
                    .then_inc(table_in[n], 16)
                if n == 1:
                    for par in range(2):
                        sp.dma_start(X[par][:, 0, :], dense[par * TB:(par + 1) * TB, :]).then_inc(dense_in[par], 16)
            sp.dma_start(w_dense_sb[:], w_dense).then_inc(wd_in, 16)
            sp.dma_start(w_pairs_sb[:], w_pairs).then_inc(w1_in, 16)
            sp.dma_start(w2_sb[:], w2).then_inc(rest_in, 16)
            sp.dma_start(w3_sb[:], w3).then_inc(rest_in, 16)
            sp.dma_start(b1_sb[:], b1).then_inc(rest_in, 16)
            sp.dma_start(b2_sb[:], b2).then_inc(rest_in, 16)
            for t in range(2, T):
                sp.wait_ge(transposed[0], NG // 2 * (t - 2) + 1)
                sp.dma_start(X[t % 2][:, 0, :], dense[t * TB:(t + 1) * TB, :]).then_inc(dense_in[t % 2], 16)
            sp.wait_ge(y_ready, T)
            sp.dma_start(out.rearrange("b o -> o b"), y[:]).then_inc(stored, 16)
            sp.wait_ge(stored, 16)

        @block.gpsimd
        def _(pool):
            pool.iota(rows_i[:], [[1, RC]], base=0, channel_multiplier=RC).then_inc(rows_made, 1)
            pool.memset(ident[:], 0.0).then_inc(zeroed, 1)
            pool.wait_ge(zeroed, 1)
            pool.affine_select(out=ident[:], in_=ident[:], compare_op=ALU.not_equal, fill=1.0, base=0,
                               pattern=[[-1, P]], channel_multiplier=1).then_inc(ident_ready, 1)
            pool.wait_ge(ids_in, 16)
            for t in range(T):
                for g, (x0, n) in enumerate(GROUPS):
                    if t >= 2:
                        pool.wait_ge(transposed[g % 2], NG // 2 * (t - 2) + g // 2 + 1)
                    for x in range(max(x0, 1), x0 + n):
                        f = GAT[x - 1]
                        at = ids_sb[:, t, f:f + 1].bitcast(U32)
                        pool.indirect_dma_start(X[t % 2][:, x, :], None, tables[f], bass.IndirectOffsetOnAxis(at, 0)) \
                            .then_inc(gathered[t % 2][g], 16)

        @block.vector
        def _(dve):
            def copy_transposed(t, g):
                dve.wait_ge(transposed[0], NG // 2 * t + g // 2 + 1)
                if g == 0:
                    dve.tensor_copy(denseT[t % 2][:], pT[0][:, 0, :])
                copy_group(dve.tensor_copy, g).then_inc(xt_copied[0], 1)

            dve.wait_ge(rows_made, 1)
            dve.tensor_copy(rows[:], rows_i[:]).then_inc(rows_ready, 1)
            dve.memset(XT[:, :, F:FP], 0.0).then_inc(pads_ready, 1)
            dve.memset(Z[:, M - 1, :], 0.0).then_inc(pads_ready, 1)
            dve.wait_ge(rows_ready, 1)
            for n in range(NS):
                dve.wait_ge(picks_in[n], 16)
                if n >= 2:
                    dve.wait_ge(picked_done, n - 1)
                for c in range(ACT_ROWS, RC):
                    last = dve.tensor_scalar(onehot[n % 2][:, c, :], picks_sb[n][0:RP, :], rows[0:RP, c:c + 1], None,
                                             ALU.is_equal)
                last.then_inc(onehot_dve, 1)
                dve.wait_ge(hi_ready, n + 1)
                dve.tensor_tensor(t_lo[n % 2][:], table[n][:], t_hi[n % 2][:].bitcast(F32),
                                  ALU.subtract).then_inc(lo_ready, 1)
                for g in FIRST[n][::2]:
                    copy_transposed(0, g)
            dve.wait_ge(wd_in, 16)
            dve.tensor_tensor(wd[:], w_dense_sb[:, 0, :], w_dense_sb[:, 1, :], ALU.add).then_inc(wd_ready, 1)
            dve.wait_ge(pads_ready, 2)
            for t in range(T):
                for r in range(NR):
                    dve.wait_ge(gram_done[r % 2], NR // 2 * t + r // 2 + 1)
                    copy_granule(dve.tensor_copy, r, (0, 1)).then_inc(z_dve[r % 2], 1)
                if t + 1 < T:
                    copy_transposed(t + 1, 0)
                dve.wait_ge(l1_done[0], t + 1)
                for n in range(N1 - 1):
                    last = dve.tensor_scalar(h1[:, n, :], p1[0][:, n, :], b1_sb[:, n:n + 1], 0.0, ALU.add, ALU.max)
                last.then_inc(h1_ready[0], 1)
                if t + 1 < T:
                    copy_transposed(t + 1, 2)
                dve.wait_ge(l2_done[1], t + 1)
                dve.tensor_scalar(h2[:, 1, :], p2[1], b2_sb[:, 1:2], 0.0, ALU.add, ALU.max).then_inc(h2_ready[1], 1)
                if t + 1 < T:
                    copy_transposed(t + 1, 4)

        @block.scalar
        def _(act):
            def copy_transposed(t, g):
                act.wait_ge(transposed[1], NG // 2 * t + g // 2 + 1)
                copy_group(act.copy, g).then_inc(xt_copied[1], 1)

            def copy_picked(t):
                act.copy(XT[:, :, 0:NS].rearrange("p b f -> p f b"), picked[:, :, t * TB:(t + 1) * TB]) \
                    .then_inc(xt_picked, 1)

            act.wait_ge(rows_made, 1)
            act.activation(rows_neg[:], rows_i[:], ACT.Copy, scale=-1.0).then_inc(rows_neg_ready, 1)
            act.wait_ge(rows_neg_ready, 1)
            for n in range(NS):
                act.wait_ge(picks_in[n], 16)
                if n >= 2:
                    act.wait_ge(onehot_act, n - 1)
                for c in range(ACT_ROWS):
                    last = act.activation(away[n % 2][:, c, :], picks_sb[n][0:RP, :], ACT.Abs,
                                          bias=rows_neg[0:RP, c:c + 1])
                last.then_inc(away_ready, 1)
                act.wait_ge(table_in[n], 16)
                if n >= 2:
                    act.wait_ge(picked_done, n - 1)
                act.copy(t_hi[n % 2][:], table[n][:]).then_inc(hi_ready, 1)
                act.wait_ge(away_ready, n + 1)
                act.activation(onehot[n % 2][:, 0:ACT_ROWS, :], away[n % 2][:], ACT.Relu, bias=1.0, scale=-1.0) \
                    .then_inc(onehot_act, 1)
                if n >= 1:
                    act.wait_ge(picked_done, n)
                    act.copy(picked[:, n - 1, :], pG[(n - 1) % 2][:, 0, :]).then_inc(picked_ready, 1)
                for g in FIRST[n][1::2]:
                    copy_transposed(0, g)
            act.wait_ge(picked_done, NS)
            act.copy(picked[:, NS - 1, :], pG[(NS - 1) % 2][:, 0, :]).then_inc(picked_ready, 1)
            act.wait_ge(picked_ready, NS)
            copy_picked(0)
            act.wait_ge(pads_ready, 2)
            act.wait_ge(rest_in, 64)
            for t in range(T):
                for r in range(NR):
                    act.wait_ge(gram_done[r % 2], NR // 2 * t + r // 2 + 1)
                    copy_granule(act.copy, r, (2, 3)).then_inc(z_act[r % 2], 1)
                if t + 1 < T:
                    copy_transposed(t + 1, 1)
                    copy_picked(t + 1)
                act.wait_ge(l1_done[1], t + 1)
                act.activation(h1[:, N1 - 1, :], p1[1][:, 0, :], ACT.Relu, bias=b1_sb[:, N1 - 1:N1]) \
                    .then_inc(h1_ready[1], 1)
                if t + 1 < T:
                    copy_transposed(t + 1, 3)
                act.wait_ge(l2_done[0], t + 1)
                act.activation(h2[:, 0, :], p2[0], ACT.Relu, bias=b2_sb[:, 0:1]).then_inc(h2_ready[0], 1)
                if t + 1 < T:
                    copy_transposed(t + 1, 5)
                act.wait_ge(l3_done, t + 1)
                act.copy(y[:, t * TB:(t + 1) * TB], pY).then_inc(y_ready, 1)

        @block.tensor
        def _(pe):
            def transpose_group(t, g):
                x, n = GROUPS[g]
                if g == 0:
                    pe.wait_ge(dense_in[t % 2], 16 * (t // 2 + 1))
                pe.wait_ge(gathered[t % 2][g], 16 * (n - (g == 0)) * (t // 2 + 1))
                if NG * t + g >= 2:
                    pe.wait_ge(xt_copied[g % 2], NG // 2 * t + g // 2)
                for f in range(n):
                    last = pe.transpose(pT[g % 2][:, f, :], X[t % 2][:, x + f, :], ident[:])
                last.then_inc(transposed[g % 2], 1)

            def gram(t):
                for k in range(2):
                    pe.wait_ge(xt_copied[k], NG // 2 * (t + 1))
                pe.wait_ge(xt_picked, t + 1)
                for r in range(NR):
                    s = r % 2
                    if NR * t + r >= 2:
                        pe.wait_ge(z_dve[s], NR // 2 * t + r // 2)
                        pe.wait_ge(z_act[s], NR // 2 * t + r // 2)
                    if r == 1 and t >= 1:
                        pe.wait_ge(y_ready, t)
                    for u in range(GK * GU):
                        b = r * GS + u * Q
                        last = pe.matmul(pG[s][:, u // GU, u % GU * GC:(u % GU + 1) * GC],
                                         XT[:, b:b + Q, :].rearrange("p b f -> p (b f)"),
                                         XT[:, b:b + Q, 1:F], start=True, stop=True)
                    last.then_inc(gram_done[s], 1)

            def layer1_dense(t):
                if t >= 1:
                    for k in range(2):
                        pe.wait_ge(h1_ready[k], t)
                for n in range(N1):
                    pe.matmul(p1[n // (N1 - 1)][:, n % (N1 - 1), :], wd[:, n * P:(n + 1) * P], denseT[t % 2][:],
                              start=(n in (0, N1 - 1)), stop=False, skip_group_check=True)

            def layer1_pairs(t):
                for s in range(2):
                    pe.wait_ge(z_dve[s], NR // 2 * (t + 1))
                    pe.wait_ge(z_act[s], NR // 2 * (t + 1))
                for n in range(N1):
                    for m in range(M):
                        last = pe.matmul(p1[n // (N1 - 1)][:, n % (N1 - 1), :],
                                         w_pairs_sb[:, m, n * P:(n + 1) * P], Z[:, m, :],
                                         start=False, stop=(m == M - 1), skip_group_check=True)
                    if n >= N1 - 2:
                        last.then_inc(l1_done[n - (N1 - 2)], 1)

            def layer2(t):
                pe.wait_ge(h1_ready[0], t + 1)
                for m in range(N1):
                    if m == N1 - 1:
                        pe.wait_ge(h1_ready[1], t + 1)
                    for n in range(N2):
                        last = pe.matmul(p2[n], w2_sb[:, m, n * P:(n + 1) * P], h1[:, m, :],
                                         start=(m == 0), stop=(m == N1 - 1))
                        if m == N1 - 1:
                            last.then_inc(l2_done[n], 1)

            def layer3(t):
                for n in range(N2):
                    pe.wait_ge(h2_ready[n], t + 1)
                    last = pe.matmul(pY, w3_sb[:, n:n + 1], h2[:, n, :], start=(n == 0), stop=(n == N2 - 1))
                last.then_inc(l3_done, 1)

            pe.wait_ge(ident_ready, 1)
            for n in range(NS):
                pe.wait_ge(onehot_act, n + 1)
                pe.wait_ge(onehot_dve, n + 1)
                pe.wait_ge(lo_ready, n + 1)
                if n >= 2:
                    pe.wait_ge(picked_ready, n - 1)
                for c in range(RC):
                    pe.matmul(pG[n % 2][:, 0, :], t_hi[n % 2][:, c, :], onehot[n % 2][:, c, :],
                              start=(c == 0), stop=False)
                    last = pe.matmul(pG[n % 2][:, 0, :], t_lo[n % 2][:, c, :], onehot[n % 2][:, c, :],
                                     start=False, stop=(c == RC - 1))
                last.then_inc(picked_done, 1)
                for g in FIRST[n]:
                    transpose_group(0, g)
            pe.wait_ge(pads_ready, 2)
            pe.wait_ge(wd_ready, 1)
            pe.wait_ge(w1_in, 16)
            pe.wait_ge(rest_in, 64)
            for t in range(T):
                gram(t)
                if t + 1 < T:
                    transpose_group(t + 1, 0)
                    transpose_group(t + 1, 1)
                layer1_dense(t)
                layer1_pairs(t)
                if t + 1 < T:
                    transpose_group(t + 1, 2)
                    transpose_group(t + 1, 3)
                layer2(t)
                if t + 1 < T:
                    transpose_group(t + 1, 4)
                    transpose_group(t + 1, 5)
                layer3(t)


def kernel(**inputs):
    import numpy as np
    import concourse.bacc as bacc
    from concourse.bass_utils import run_bass_kernel_spmd

    ids = np.asarray(inputs["ids"])
    w1 = np.asarray(inputs["W_top1"])
    B = ids.shape[0]
    none = w1.shape[0]
    row = np.full((P, M), none)
    for g in range(1, F):
        for f in range(g):
            m, q = divmod(g - 1, Q)
            a, b = sorted((SLOTS[f], SLOTS[g]))
            row[32 * q + f, m] = D + a * (2 * F - a - 1) // 2 + b - a - 1
    padded = np.concatenate([w1, np.zeros((1, H1), w1.dtype)])
    arrays = {
        "dense": np.asarray(inputs["r_dense_features"]),
        "ids": ids,
        "picks": ids[:, SEL].T,
        "w_dense": np.stack([w1[0:D], w1[none - D:none]], axis=1),
        "w_pairs": padded[row],
        "w2": np.asarray(inputs["W_top2"]).reshape(N1, P, H2).transpose(1, 0, 2),
        "w3": np.asarray(inputs["W_top3"]).reshape(N2, P).T,
        "b1": np.asarray(inputs["b_top1"]).reshape(N1, P).T,
        "b2": np.asarray(inputs["b_top2"]).reshape(N2, P).T,
    }
    for f in range(NT):
        arrays[f"tbl_{f}"] = np.asarray(inputs[f"tbl_{f}"])
    arrays = {f"in_{k}": np.ascontiguousarray(a) for k, a in arrays.items()}
    nc = bacc.Bacc("TRN2", target_bir_lowering=False, num_devices=1)
    ap = {k[3:]: nc.dram_tensor(k, a.shape, mybir.dt.from_np(a.dtype), kind="ExternalInput").ap()
          for k, a in arrays.items()}
    out = nc.dram_tensor("out_y", (B, 1), F32, kind="ExternalOutput").ap()
    dlrm_tower(nc, ap["dense"], ap["ids"], ap["picks"], [ap[f"tbl_{f}"] for f in range(NT)], ap["w_dense"],
               ap["w_pairs"], ap["w2"], ap["w3"], ap["b1"], ap["b2"], out)
    return run_bass_kernel_spmd(nc, [arrays], core_ids=[0]).results[0]["out_y"]
```

```python
from contextlib import ExitStack

import concourse.bass as bass
from concourse import mybir

P = 128
NT = 26
F = NT + 1
BLK = 4
NB = -(-F // BLK)
FP = NB * BLK
D = 128
TB = 128
H1, H2 = 512, 256
N1, N2 = H1 // P, H2 // P

SEL = [1, 5, 7, 12, 15, 20, 21, 22, 23]
NS = len(SEL)
GAT = [f for f in range(NT) if f not in SEL]
RP, RC = 125, 8
TBUF = 6
NBUF = 3
ACT_ROWS = 2
SLOTS = [1 + f for f in SEL] + [0] + [1 + f for f in GAT]

Q = 4
SQ = TB // Q
HALVES = 2
SH = SQ // HALVES

BLOCKS = [[0, 0, 0, 0, 4, 4, 4],
          [4, 1, 1, 1, 1, 5, 5],
          [5, 5, 2, 2, 2, 2, 6],
          [6, 6, 6, 3, 3, 3, 3]]
assert sorted(sorted((BLOCKS[q][r], r)) for q in range(Q) for r in range(NB)) == \
    [[r, i] for r in range(NB) for i in range(r, NB)]


def block_copies(level):
    copies = []
    for q in range(Q):
        ends = [r + 1 for r in range(NB) if r + 1 == NB or BLOCKS[q][r + 1] != BLOCKS[q][r]][::-1]
        if level < len(ends):
            copies.append((q, BLK * ends[level], BLOCKS[q][ends[level] - 1]))
    return copies


LEVELS = 3
assert block_copies(LEVELS - 1) and not block_copies(LEVELS)
STEPS_DVE = [(0, 0), (0, 1), (1, 0), (1, 1), (2, 0)]
STEPS_ACT = [(0, 2), (0, 3), (1, 2), (1, 3), (2, 2), (2, 3), (2, 1)]
assert sorted(STEPS_DVE + STEPS_ACT) == [(level, j) for level in range(LEVELS) for j in range(Q)]

TG = 4
NX = 1 + len(GAT)
NG = 6
SIZES = [NX // NG + (g < NX % NG) for g in range(NG)]
GROUPS = [(sum(SIZES[:g]), SIZES[g]) for g in range(NG)]
assert max(SIZES) <= TG and NG % 2 == 0

ALU = mybir.AluOpType
ACT = mybir.ActivationFunctionType
F32 = mybir.dt.float32
F32R = mybir.dt.float32r
I32 = mybir.dt.int32
U32 = mybir.dt.uint32


def dlrm_tower(nc, dense, ids, picks, tables, w_dense, w_pairs, w2, w3, b1, b2, out):
    B = dense.shape[0]
    T = B // TB
    with ExitStack() as ctx:
        def sb(name, shape, dt=F32):
            return ctx.enter_context(nc.sbuf_tensor(name, shape, dt))

        def ps(name, shape):
            return ctx.enter_context(nc.psum_tensor(name, shape, F32))

        def sem(name):
            return ctx.enter_context(nc.semaphore(name))

        picks_sb = [sb(f"picks{n}_sb", [P, B], I32) for n in range(NS)]
        table = [sb(f"table{n}", [RP, RC, D]) for n in range(TBUF)]
        t_hi = [sb(f"t_hi{n}", [RP, RC, D], F32R) for n in range(NBUF)]
        t_lo = [sb(f"t_lo{n}", [RP, RC, D], F32R) for n in range(NBUF)]
        onehot = [sb(f"onehot{n}", [RP, RC, B], F32R) for n in range(NBUF)]
        away = [sb(f"away{n}", [RP, ACT_ROWS, B]) for n in range(2)]
        rows_i = sb("rows_i", [P, RC], I32)
        rows = sb("rows", [P, RC])
        rows_neg = sb("rows_neg", [P, RC])
        picked = sb("picked", [P, NS, B])
        ids_sb = sb("ids_sb", [P, T, NT], I32)
        X = [sb(f"X{i}", [P, NX, D]) for i in range(2)]
        XT = sb("XT", [P, TB, FP])
        denseT = [sb(f"denseT{i}", [P, TB]) for i in range(2)]
        Z = sb("Z", [P, BLK, TB])
        h1 = sb("h1", [P, N1, TB])
        h2 = sb("h2", [P, N2, TB])
        y = sb("y", [1, B])
        w_dense_sb = sb("w_dense_sb", [P, 2, H1])
        wd = sb("wd", [P, H1])
        w_pairs_sb = sb("w_pairs_sb", [P, BLK, H1])
        w2_sb = sb("w2_sb", [P, N1, H2])
        w3_sb = sb("w3_sb", [P, N2])
        b1_sb = sb("b1_sb", [P, N1])
        b2_sb = sb("b2_sb", [P, N2])
        ident = sb("ident", [P, P])

        pT = [ps(f"pT{k}", [P, TG, TB]) for k in range(2)]
        pG = [ps(f"pG{s}", [P, 512]) for s in range(2)]
        p1 = [ps("p1_first", [P, N1 - 1, TB]), ps("p1_last", [P, 1, TB])]
        p2 = [ps(f"p2_{n}", [P, 512]) for n in range(N2)]
        p_picked = [[p2[1], pG[0], pG[1]][(NS - 1 - n) % 3] for n in range(NS)]
        pY = p2[0][0:1, 0:TB]

        ids_in = sem("ids_in")
        dense_in = [sem(f"dense_in{i}") for i in range(2)]
        gathered = [[sem(f"gathered{i}_{g}") for g in range(NG)] for i in range(2)]
        picks_in = [sem(f"picks_in{n}") for n in range(NS)]
        table_in = [sem(f"table_in{n}") for n in range(NS)]
        wd_in = sem("wd_in")
        w1_in = sem("w1_in")
        rest_in = sem("rest_in")
        zeroed = sem("zeroed")
        ident_ready = sem("ident_ready")
        rows_made = sem("rows_made")
        rows_ready = sem("rows_ready")
        rows_neg_ready = sem("rows_neg_ready")
        pads_ready = sem("pads_ready")
        wd_ready = sem("wd_ready")
        hi_ready = sem("hi_ready")
        away_ready = sem("away_ready")
        onehot_dve = sem("onehot_dve")
        onehot_act = sem("onehot_act")
        lo_ready = sem("lo_ready")
        picked_done = sem("picked_done")
        picked_ready = sem("picked_ready")
        xt_picked = sem("xt_picked")
        transposed = [sem(f"transposed{k}") for k in range(2)]
        xt_copied = [sem(f"xt_copied{k}") for k in range(2)]
        gram_done = [sem(f"gram_done{s}") for s in range(2)]
        z_dve = sem("z_dve")
        z_act = sem("z_act")
        l1_done = [sem("l1_first_done"), sem("l1_last_done")]
        h1_ready = [sem("h1_first_ready"), sem("h1_last_ready")]
        l2_done = [sem(f"l2_done{n}") for n in range(N2)]
        h2_ready = [sem(f"h2_ready{n}") for n in range(N2)]
        l3_done = sem("l3_done")
        y_ready = sem("y_ready")
        stored = sem("stored")

        def copy_products(copy, s, level, j):
            src = pG[s][32 * j:32 * j + FP, 0:SH * FP].rearrange("p (b c) -> p c b", c=FP)
            b = j * SQ + s * SH
            for q, end, i in block_copies(level):
                last = copy(Z[32 * q:32 * q + end, :, b:b + SH], src[0:end, BLK * i:BLK * i + BLK, :])
            return last

        def copy_group(copy, g):
            x, n = GROUPS[g]
            return copy(XT[:, :, NS + x:NS + x + n].rearrange("p b f -> p f b"), pT[g % 2][:, 0:n, :])

        block = ctx.enter_context(nc.Block())

        @block.sync
        def _(sp):
            sp.dma_start(ids_sb[:], ids.rearrange("(t p) f -> p t f", p=TB)).then_inc(ids_in, 16)
            for n in range(NS):
                sp.dma_start(picks_sb[n][:], picks[n, :].partition_broadcast(P)).then_inc(picks_in[n], 16)
                if n >= 1:
                    if n >= TBUF:
                        sp.wait_ge(lo_ready, n - TBUF + 1)
                    sp.dma_start(table[n % TBUF][:], tables[SEL[n]].rearrange("(p c) d -> p c d", c=RC)) \
                        .then_inc(table_in[n], 16)
                if n == 1:
                    for par in range(2):
                        sp.dma_start(X[par][:, 0, :], dense[par * TB:(par + 1) * TB, :]).then_inc(dense_in[par], 16)
            sp.dma_start(w_dense_sb[:], w_dense).then_inc(wd_in, 16)
            sp.dma_start(w_pairs_sb[:], w_pairs).then_inc(w1_in, 16)
            sp.dma_start(w2_sb[:], w2).then_inc(rest_in, 16)
            sp.dma_start(w3_sb[:], w3).then_inc(rest_in, 16)
            sp.dma_start(b1_sb[:], b1).then_inc(rest_in, 16)
            sp.dma_start(b2_sb[:], b2).then_inc(rest_in, 16)
            for t in range(2, T):
                sp.wait_ge(transposed[0], NG // 2 * (t - 2) + 1)
                sp.dma_start(X[t % 2][:, 0, :], dense[t * TB:(t + 1) * TB, :]).then_inc(dense_in[t % 2], 16)
            sp.wait_ge(y_ready, T)
            sp.dma_start(out.rearrange("b o -> o b"), y[:]).then_inc(stored, 16)
            sp.wait_ge(stored, 16)

        @block.gpsimd
        def _(pool):
            pool.iota(rows_i[:], [[1, RC]], base=0, channel_multiplier=RC).then_inc(rows_made, 1)
            pool.memset(ident[:], 0.0).then_inc(zeroed, 1)
            pool.wait_ge(zeroed, 1)
            pool.affine_select(out=ident[:], in_=ident[:], compare_op=ALU.not_equal, fill=1.0, base=0,
                               pattern=[[-1, P]], channel_multiplier=1).then_inc(ident_ready, 1)
            pool.wait_ge(ids_in, 16)
            for t in range(T):
                for g, (x0, n) in enumerate(GROUPS):
                    if t >= 2:
                        pool.wait_ge(transposed[g % 2], NG // 2 * (t - 2) + g // 2 + 1)
                    for x in range(max(x0, 1), x0 + n):
                        f = GAT[x - 1]
                        at = ids_sb[:, t, f:f + 1].bitcast(U32)
                        pool.indirect_dma_start(X[t % 2][:, x, :], None, tables[f], bass.IndirectOffsetOnAxis(at, 0)) \
                            .then_inc(gathered[t % 2][g], 16)

        @block.vector
        def _(dve):
            def copy_transposed(t, g):
                dve.wait_ge(transposed[0], NG // 2 * t + g // 2 + 1)
                if g == 0:
                    dve.tensor_copy(denseT[t % 2][:], pT[0][:, 0, :])
                copy_group(dve.tensor_copy, g).then_inc(xt_copied[0], 1)

            def relu_h2(t):
                dve.wait_ge(l2_done[1], t + 1)
                dve.tensor_scalar(h2[:, 1, :], p2[1][:, 0:TB], b2_sb[:, 1:2], 0.0, ALU.add, ALU.max) \
                    .then_inc(h2_ready[1], 1)

            dve.wait_ge(rows_made, 1)
            dve.tensor_copy(rows[:], rows_i[:]).then_inc(rows_ready, 1)
            dve.memset(XT[:, :, F:FP], 0.0).then_inc(pads_ready, 1)
            dve.memset(Z[:], 0.0).then_inc(pads_ready, 1)
            dve.wait_ge(rows_ready, 1)
            for n in range(NS):
                dve.wait_ge(picks_in[n], 16)
                if n >= NBUF:
                    dve.wait_ge(picked_done, n - NBUF + 1)
                for c in range(ACT_ROWS, RC):
                    if c == ACT_ROWS + 2:
                        dve.wait_ge(hi_ready, n + 1)
                        dve.tensor_tensor(t_lo[n % NBUF][:], table[n % TBUF][:], t_hi[n % NBUF][:].bitcast(F32),
                                          ALU.subtract).then_inc(lo_ready, 1)
                    dve.tensor_scalar(onehot[n % NBUF][:, c, :], picks_sb[n][0:RP, :], rows[0:RP, c:c + 1], None,
                                      ALU.is_equal).then_inc(onehot_dve, 1)
            for g in range(0, NG, 2):
                copy_transposed(0, g)
            dve.wait_ge(wd_in, 16)
            dve.tensor_tensor(wd[:], w_dense_sb[:, 0, :], w_dense_sb[:, 1, :], ALU.add).then_inc(wd_ready, 1)
            dve.wait_ge(pads_ready, 2)
            for t in range(T):
                for s in range(HALVES):
                    dve.wait_ge(gram_done[s], t + 1)
                    done = (t * HALVES + s) * len(STEPS_DVE)
                    for level, j in STEPS_DVE:
                        if level >= 1:
                            dve.wait_ge(z_dve, done + STEPS_DVE.index((level - 1, j)) + 1)
                        copy_products(dve.tensor_copy, s, level, j).then_inc(z_dve, 1)
                if t >= 1:
                    relu_h2(t - 1)
                if t + 1 < T:
                    for g in range(0, NG, 2):
                        copy_transposed(t + 1, g)
                dve.wait_ge(l1_done[0], t + 1)
                for n in range(N1 - 1):
                    last = dve.tensor_scalar(h1[:, n, :], p1[0][:, n, :], b1_sb[:, n:n + 1], 0.0, ALU.add, ALU.max)
                last.then_inc(h1_ready[0], 1)
            relu_h2(T - 1)

        @block.scalar
        def _(act):
            def copy_transposed(t, g):
                act.wait_ge(transposed[1], NG // 2 * t + g // 2 + 1)
                copy_group(act.copy, g).then_inc(xt_copied[1], 1)

            def copy_product(n):
                act.wait_ge(picked_done, n + 1)
                act.copy(picked[:, n, :], p_picked[n][:]).then_inc(picked_ready, 1)

            def copy_picked(t):
                act.copy(XT[:, :, 0:NS].rearrange("p b f -> p f b"), picked[:, :, t * TB:(t + 1) * TB]) \
                    .then_inc(xt_picked, 1)

            def relu_h2(t):
                act.wait_ge(l2_done[0], t + 1)
                act.activation(h2[:, 0, :], p2[0][:, 0:TB], ACT.Relu, bias=b2_sb[:, 0:1]).then_inc(h2_ready[0], 1)

            def copy_y(t):
                act.wait_ge(l3_done, t + 1)
                act.copy(y[:, t * TB:(t + 1) * TB], pY).then_inc(y_ready, 1)

            act.dma_start(table[0][:], tables[SEL[0]].rearrange("(p c) d -> p c d", c=RC)).then_inc(table_in[0], 16)
            act.wait_ge(rows_made, 1)
            act.activation(rows_neg[:], rows_i[:], ACT.Copy, scale=-1.0).then_inc(rows_neg_ready, 1)
            act.wait_ge(rows_neg_ready, 1)
            for n in range(NS):
                act.wait_ge(table_in[n], 16)
                if n >= NBUF:
                    act.wait_ge(picked_done, n - NBUF + 1)
                act.copy(t_hi[n % NBUF][:], table[n % TBUF][:]).then_inc(hi_ready, 1)
                act.wait_ge(picks_in[n], 16)
                if n >= 2:
                    act.wait_ge(onehot_act, n - 1)
                for c in range(ACT_ROWS):
                    last = act.activation(away[n % 2][:, c, :], picks_sb[n][0:RP, :], ACT.Abs,
                                          bias=rows_neg[0:RP, c:c + 1])
                last.then_inc(away_ready, 1)
                if n >= 2:
                    copy_product(n - 2)
                act.wait_ge(away_ready, n + 1)
                act.activation(onehot[n % NBUF][:, 0:ACT_ROWS, :], away[n % 2][:], ACT.Relu, bias=1.0, scale=-1.0) \
                    .then_inc(onehot_act, 1)
            copy_product(NS - 2)
            copy_transposed(0, 1)
            act.wait_ge(picked_ready, NS - 1)
            act.copy(XT[:, :, 0:NS - 1].rearrange("p b f -> p f b"), picked[:, 0:NS - 1, 0:TB]).then_inc(xt_picked, 1)
            for g in range(3, NG, 2):
                copy_transposed(0, g)
            act.wait_ge(picked_done, NS)
            act.copy(XT[:, :, NS - 1], p_picked[NS - 1][:, 0:TB]).then_inc(xt_picked, 1)
            copy_product(NS - 1)
            act.wait_ge(picked_ready, NS)
            act.wait_ge(pads_ready, 2)
            act.wait_ge(rest_in, 64)
            for t in range(T):
                for s in range(HALVES):
                    act.wait_ge(gram_done[s], t + 1)
                    done = (t * HALVES + s) * len(STEPS_ACT)
                    done_dve = (t * HALVES + s) * len(STEPS_DVE)
                    for level, j in STEPS_ACT:
                        if (level - 1, j) in STEPS_DVE:
                            act.wait_ge(z_dve, done_dve + STEPS_DVE.index((level - 1, j)) + 1)
                        elif level >= 1:
                            act.wait_ge(z_act, done + STEPS_ACT.index((level - 1, j)) + 1)
                        copy_products(act.copy, s, level, j).then_inc(z_act, 1)
                if t >= 1:
                    relu_h2(t - 1)
                if t + 1 < T:
                    copy_picked(t + 1)
                    copy_transposed(t + 1, 1)
                if t >= 1:
                    copy_y(t - 1)
                if t + 1 < T:
                    copy_transposed(t + 1, 3)
                    copy_transposed(t + 1, 5)
                act.wait_ge(l1_done[1], t + 1)
                act.activation(h1[:, N1 - 1, :], p1[1][:, 0, :], ACT.Relu, bias=b1_sb[:, N1 - 1:N1]) \
                    .then_inc(h1_ready[1], 1)
            relu_h2(T - 1)
            copy_y(T - 1)

        @block.tensor
        def _(pe):
            def warm_up(n):
                for _ in range(n):
                    pe.matmul(p2[0][:, 0:TB], ident[:], ident[:], start=True, stop=True)

            def transpose_group(t, g):
                x, n = GROUPS[g]
                if g == 0:
                    pe.wait_ge(dense_in[t % 2], 16 * (t // 2 + 1))
                pe.wait_ge(gathered[t % 2][g], 16 * (n - (g == 0)) * (t // 2 + 1))
                if NG * t + g >= 2:
                    pe.wait_ge(xt_copied[g % 2], NG // 2 * t + g // 2)
                for f in range(n):
                    last = pe.transpose(pT[g % 2][:, f, :], X[t % 2][:, x + f, :], ident[:])
                last.then_inc(transposed[g % 2], 1)

            def gram(t):
                for k in range(2):
                    pe.wait_ge(xt_copied[k], NG // 2 * (t + 1))
                pe.wait_ge(xt_picked, t + 2)
                if t >= 1:
                    pe.wait_ge(z_dve, HALVES * len(STEPS_DVE) * t)
                    pe.wait_ge(z_act, HALVES * len(STEPS_ACT) * t)
                for s in range(HALVES):
                    for i in range(SH):
                        for j in range(Q):
                            x = XT[:, j * SQ + s * SH + i, :]
                            last = pe.matmul(pG[s][32 * j:32 * j + FP, i * FP:(i + 1) * FP], x, x,
                                             start=True, stop=True)
                    last.then_inc(gram_done[s], 1)

            def layer1_dense(t):
                if t >= 1:
                    for k in range(2):
                        pe.wait_ge(h1_ready[k], t)
                for n in range(N1):
                    pe.matmul(p1[n // (N1 - 1)][:, n % (N1 - 1), :], wd[:, n * P:(n + 1) * P], denseT[t % 2][:],
                              start=(n in (0, N1 - 1)), stop=False, skip_group_check=True)

            def layer1_pairs(t, chunks):
                if 0 in chunks:
                    pe.wait_ge(z_dve, HALVES * len(STEPS_DVE) * (t + 1))
                    pe.wait_ge(z_act, HALVES * len(STEPS_ACT) * (t + 1))
                for n in chunks:
                    for m in range(BLK):
                        last = pe.matmul(p1[n // (N1 - 1)][:, n % (N1 - 1), :],
                                         w_pairs_sb[:, m, n * P:(n + 1) * P], Z[:, m, :],
                                         start=False, stop=(m == BLK - 1), skip_group_check=True)
                    if n >= N1 - 2:
                        last.then_inc(l1_done[n - (N1 - 2)], 1)

            def layer2(t):
                pe.wait_ge(h1_ready[0], t + 1)
                if t >= 1:
                    pe.wait_ge(y_ready, t)
                for m in range(N1):
                    if m == N1 - 1:
                        pe.wait_ge(h1_ready[1], t + 1)
                    for n in range(N2):
                        last = pe.matmul(p2[n][:, 0:TB], w2_sb[:, m, n * P:(n + 1) * P], h1[:, m, :],
                                         start=(m == 0), stop=(m == N1 - 1))
                        if m == N1 - 1:
                            last.then_inc(l2_done[n], 1)

            def layer3(t):
                for n in range(N2):
                    pe.wait_ge(h2_ready[n], t + 1)
                    last = pe.matmul(pY, w3_sb[:, n:n + 1], h2[:, n, :], start=(n == 0), stop=(n == N2 - 1))
                last.then_inc(l3_done, 1)

            pe.wait_ge(ident_ready, 1)
            warm_up(10)
            for n in range(NS):
                if n >= 3:
                    pe.wait_ge(picked_ready, n - 2)
                pe.wait_ge(hi_ready, n + 1)
                for i, c0 in enumerate([*range(ACT_ROWS, RC, 2), *range(0, ACT_ROWS, 2)]):
                    for part in (t_hi, t_lo):
                        for c in (c0, c0 + 1):
                            if part is t_hi and c >= ACT_ROWS:
                                pe.wait_ge(onehot_dve, (RC - ACT_ROWS) * n + c - ACT_ROWS + 1)
                            elif part is t_hi:
                                pe.wait_ge(onehot_act, n + 1)
                            elif i == 0:
                                pe.wait_ge(lo_ready, n + 1)
                            last = pe.matmul(p_picked[n][:], part[n % NBUF][:, c, :], onehot[n % NBUF][:, c, :],
                                             start=(part is t_hi and c == ACT_ROWS),
                                             stop=(part is t_lo and c == ACT_ROWS - 1))
                    if n == NS - 1 and i < NG // 2:
                        transpose_group(0, 2 * i)
                        transpose_group(0, 2 * i + 1)
                last.then_inc(picked_done, 1)
            warm_up(2)
            pe.wait_ge(pads_ready, 2)
            pe.wait_ge(wd_ready, 1)
            pe.wait_ge(w1_in, 16)
            pe.wait_ge(rest_in, 64)
            for t in range(T):
                gram(t)
                if t + 1 < T:
                    transpose_group(t + 1, 0)
                    transpose_group(t + 1, 1)
                if t >= 1:
                    layer2(t - 1)
                layer1_dense(t)
                if t == 0:
                    warm_up(4)
                layer1_pairs(t, [0])
                if t >= 1:
                    layer3(t - 1)
                if t + 1 < T:
                    transpose_group(t + 1, 2)
                    transpose_group(t + 1, 3)
                layer1_pairs(t, [1])
                if t + 1 < T:
                    transpose_group(t + 1, 4)
                    transpose_group(t + 1, 5)
                layer1_pairs(t, [2, 3])
            layer2(T - 1)
            layer3(T - 1)


def kernel(**inputs):
    import numpy as np
    import concourse.bacc as bacc
    from concourse.bass_utils import run_bass_kernel_spmd

    ids = np.asarray(inputs["ids"])
    w1 = np.asarray(inputs["W_top1"])
    B = ids.shape[0]
    none = w1.shape[0]
    row = np.full((P, BLK), none)
    for q in range(Q):
        for f in range(F):
            for m in range(BLK):
                g = BLK * BLOCKS[q][f // BLK] + m
                if g < F and (f < g or g // BLK != f // BLK):
                    a, b = sorted((SLOTS[f], SLOTS[g]))
                    row[32 * q + f, m] = D + a * (2 * F - a - 1) // 2 + b - a - 1
    padded = np.concatenate([w1, np.zeros((1, H1), w1.dtype)])
    arrays = {
        "dense": np.asarray(inputs["r_dense_features"]),
        "ids": ids,
        "picks": ids[:, SEL].T,
        "w_dense": np.stack([w1[0:D], w1[none - D:none]], axis=1),
        "w_pairs": padded[row],
        "w2": np.asarray(inputs["W_top2"]).reshape(N1, P, H2).transpose(1, 0, 2),
        "w3": np.asarray(inputs["W_top3"]).reshape(N2, P).T,
        "b1": np.asarray(inputs["b_top1"]).reshape(N1, P).T,
        "b2": np.asarray(inputs["b_top2"]).reshape(N2, P).T,
    }
    for f in range(NT):
        arrays[f"tbl_{f}"] = np.asarray(inputs[f"tbl_{f}"])
    arrays = {f"in_{k}": np.ascontiguousarray(a) for k, a in arrays.items()}
    nc = bacc.Bacc("TRN2", target_bir_lowering=False, num_devices=1)
    ap = {k[3:]: nc.dram_tensor(k, a.shape, mybir.dt.from_np(a.dtype), kind="ExternalInput").ap()
          for k, a in arrays.items()}
    out = nc.dram_tensor("out_y", (B, 1), F32, kind="ExternalOutput").ap()
    dlrm_tower(nc, ap["dense"], ap["ids"], ap["picks"], [ap[f"tbl_{f}"] for f in range(NT)], ap["w_dense"],
               ap["w_pairs"], ap["w2"], ap["w3"], ap["b1"], ap["b2"], out)
    return run_bass_kernel_spmd(nc, [arrays], core_ids=[0]).results[0]["out_y"]
```
